# Optimizing a Trainium2 kernel written in Bass

```python
import numpy as np
import jax
import jax.numpy as jnp

def _softmax(x, axis=-1):
    return jax.nn.softmax(x, axis=axis)

def _gelu(x):
    return jax.nn.gelu(x, approximate=True)

def _silu(x):
    return jax.nn.silu(x)

def _sigmoid(x):
    return jax.nn.sigmoid(x)

def _layernorm(x, axis=-1, eps=1e-05):
    m = jnp.mean(x, axis=axis, keepdims=True)
    v = jnp.var(x, axis=axis, keepdims=True)
    return (x - m) / jnp.sqrt(v + eps)

def _scatter_add(tgt, idx, src, axis=0):
    return tgt.at[idx].add(src)

def _segment_sum(src, seg, n):
    return jax.ops.segment_sum(src, seg, n)
kernel_name = 'mk_dlrm_tower_d1_rec_r8_e173c3'

def setup_inputs(seed: int=0):
    np.random.seed(seed)
    _w = jnp.asarray

    def _rec_inputs():
        import jax
        import jax.numpy as jnp
        _tk = jax.random.key(seed)
        ids = jnp.stack([jax.random.randint(jax.random.fold_in(_tk, 200 + f), (512,), 0, v, jnp.int32) for f, v in enumerate([1250, 1250, 1250, 1250, 12500, 1250, 125000, 12500, 1250, 12500, 1250, 12500, 1000, 12500, 1000, 1250, 1250, 1250, 1000, 1000, 1250, 1250, 1000, 1250, 1250, 12500])], axis=1)
        tbl_0 = 0.05 * jax.random.normal(jax.random.fold_in(_tk, 500 + 0), (1250, 128), jnp.float32)
        tbl_1 = 0.05 * jax.random.normal(jax.random.fold_in(_tk, 500 + 1), (1250, 128), jnp.float32)
        tbl_2 = 0.05 * jax.random.normal(jax.random.fold_in(_tk, 500 + 2), (1250, 128), jnp.float32)
        tbl_3 = 0.05 * jax.random.normal(jax.random.fold_in(_tk, 500 + 3), (1250, 128), jnp.float32)
        tbl_4 = 0.05 * jax.random.normal(jax.random.fold_in(_tk, 500 + 4), (12500, 128), jnp.float32)
        tbl_5 = 0.05 * jax.random.normal(jax.random.fold_in(_tk, 500 + 5), (1250, 128), jnp.float32)
        tbl_6 = 0.05 * jax.random.normal(jax.random.fold_in(_tk, 500 + 6), (125000, 128), jnp.float32)
        tbl_7 = 0.05 * jax.random.normal(jax.random.fold_in(_tk, 500 + 7), (12500, 128), jnp.float32)
        tbl_8 = 0.05 * jax.random.normal(jax.random.fold_in(_tk, 500 + 8), (1250, 128), jnp.float32)
        tbl_9 = 0.05 * jax.random.normal(jax.random.fold_in(_tk, 500 + 9), (12500, 128), jnp.float32)
        tbl_10 = 0.05 * jax.random.normal(jax.random.fold_in(_tk, 500 + 10), (1250, 128), jnp.float32)
        tbl_11 = 0.05 * jax.random.normal(jax.random.fold_in(_tk, 500 + 11), (12500, 128), jnp.float32)
        tbl_12 = 0.05 * jax.random.normal(jax.random.fold_in(_tk, 500 + 12), (1000, 128), jnp.float32)
        tbl_13 = 0.05 * jax.random.normal(jax.random.fold_in(_tk, 500 + 13), (12500, 128), jnp.float32)
        tbl_14 = 0.05 * jax.random.normal(jax.random.fold_in(_tk, 500 + 14), (1000, 128), jnp.float32)
        tbl_15 = 0.05 * jax.random.normal(jax.random.fold_in(_tk, 500 + 15), (1250, 128), jnp.float32)
        tbl_16 = 0.05 * jax.random.normal(jax.random.fold_in(_tk, 500 + 16), (1250, 128), jnp.float32)
        tbl_17 = 0.05 * jax.random.normal(jax.random.fold_in(_tk, 500 + 17), (1250, 128), jnp.float32)
        tbl_18 = 0.05 * jax.random.normal(jax.random.fold_in(_tk, 500 + 18), (1000, 128), jnp.float32)
        tbl_19 = 0.05 * jax.random.normal(jax.random.fold_in(_tk, 500 + 19), (1000, 128), jnp.float32)
        tbl_20 = 0.05 * jax.random.normal(jax.random.fold_in(_tk, 500 + 20), (1250, 128), jnp.float32)
        tbl_21 = 0.05 * jax.random.normal(jax.random.fold_in(_tk, 500 + 21), (1250, 128), jnp.float32)
        tbl_22 = 0.05 * jax.random.normal(jax.random.fold_in(_tk, 500 + 22), (1000, 128), jnp.float32)
        tbl_23 = 0.05 * jax.random.normal(jax.random.fold_in(_tk, 500 + 23), (1250, 128), jnp.float32)
        tbl_24 = 0.05 * jax.random.normal(jax.random.fold_in(_tk, 500 + 24), (1250, 128), jnp.float32)
        tbl_25 = 0.05 * jax.random.normal(jax.random.fold_in(_tk, 500 + 25), (12500, 128), jnp.float32)
        _rk = jax.random.fold_in(_tk, 7)
        r_dense_features = -0.000520686 + 1.00062 * jax.random.normal(jax.random.fold_in(_rk, 101), (512, 128), jnp.float32)
        W_top1 = 0.0405887 * jax.random.normal(jax.random.fold_in(_tk, 801), (607, 512), jnp.float32)
        W_top2 = 0.0441942 * jax.random.normal(jax.random.fold_in(_tk, 802), (512, 256), jnp.float32)
        W_top3 = 0.0625 * jax.random.normal(jax.random.fold_in(_tk, 803), (256, 1), jnp.float32)
        b_top1 = jnp.zeros((512,), jnp.float32)
        b_top2 = jnp.zeros((256,), jnp.float32)
        return (r_dense_features, ids, tbl_0, tbl_1, tbl_2, tbl_3, tbl_4, tbl_5, tbl_6, tbl_7, tbl_8, tbl_9, tbl_10, tbl_11, tbl_12, tbl_13, tbl_14, tbl_15, tbl_16, tbl_17, tbl_18, tbl_19, tbl_20, tbl_21, tbl_22, tbl_23, tbl_24, tbl_25, W_top1, b_top1, W_top2, b_top2, W_top3)
    r_dense_features, ids, tbl_0, tbl_1, tbl_2, tbl_3, tbl_4, tbl_5, tbl_6, tbl_7, tbl_8, tbl_9, tbl_10, tbl_11, tbl_12, tbl_13, tbl_14, tbl_15, tbl_16, tbl_17, tbl_18, tbl_19, tbl_20, tbl_21, tbl_22, tbl_23, tbl_24, tbl_25, W_top1, b_top1, W_top2, b_top2, W_top3 = _rec_inputs()

    def _L0_rec_setup():
        import jax, jax.numpy as jnp
        import numpy as np
        NUM_SPARSE = 26
        EMBED_DIM = 128
        BATCH = 2048
        key = jax.random.key(seed)
        k1, k2 = jax.random.split(key)
        dense_features = jax.random.normal(k1, (BATCH, EMBED_DIM), dtype=jnp.float32)
        sparse_features = jax.random.normal(k2, (BATCH, NUM_SPARSE, EMBED_DIM), dtype=jnp.float32)
        return {'dense_features': dense_features, 'sparse_features': sparse_features}
    _L0_rec_all = _L0_rec_setup()
    _L0_rec_in = {k: v for k, v in _L0_rec_all.items() if k in ()}
    del _L0_rec_all
    return {'r_dense_features': r_dense_features, 'ids': ids, 'tbl_0': tbl_0, 'tbl_1': tbl_1, 'tbl_2': tbl_2, 'tbl_3': tbl_3, 'tbl_4': tbl_4, 'tbl_5': tbl_5, 'tbl_6': tbl_6, 'tbl_7': tbl_7, 'tbl_8': tbl_8, 'tbl_9': tbl_9, 'tbl_10': tbl_10, 'tbl_11': tbl_11, 'tbl_12': tbl_12, 'tbl_13': tbl_13, 'tbl_14': tbl_14, 'tbl_15': tbl_15, 'tbl_16': tbl_16, 'tbl_17': tbl_17, 'tbl_18': tbl_18, 'tbl_19': tbl_19, 'tbl_20': tbl_20, 'tbl_21': tbl_21, 'tbl_22': tbl_22, 'tbl_23': tbl_23, 'tbl_24': tbl_24, 'tbl_25': tbl_25, 'W_top1': W_top1, 'b_top1': b_top1, 'W_top2': W_top2, 'b_top2': b_top2, 'W_top3': W_top3}

def reference(r_dense_features, ids, tbl_0, tbl_1, tbl_2, tbl_3, tbl_4, tbl_5, tbl_6, tbl_7, tbl_8, tbl_9, tbl_10, tbl_11, tbl_12, tbl_13, tbl_14, tbl_15, tbl_16, tbl_17, tbl_18, tbl_19, tbl_20, tbl_21, tbl_22, tbl_23, tbl_24, tbl_25, W_top1, b_top1, W_top2, b_top2, W_top3):
    import jax
    import jax.numpy as jnp

    def _L0_rec_ref(dense_features, sparse_features):
        import jax, jax.numpy as jnp
        import numpy as np
        NUM_SPARSE = 26
        EMBED_DIM = 128
        BATCH = 2048
        F = NUM_SPARSE + 1
        combined = jnp.concatenate([dense_features[:, None, :], sparse_features], axis=1)
        interactions = jnp.einsum('bfd,bgd->bfg', combined, combined)
        iu, ju = jnp.triu_indices(F, k=1)
        interactions_flat = interactions[:, iu, ju]
        return jnp.concatenate([dense_features, interactions_flat], axis=1)
    e = jnp.stack([tbl_0[ids[:, 0]], tbl_1[ids[:, 1]], tbl_2[ids[:, 2]], tbl_3[ids[:, 3]], tbl_4[ids[:, 4]], tbl_5[ids[:, 5]], tbl_6[ids[:, 6]], tbl_7[ids[:, 7]], tbl_8[ids[:, 8]], tbl_9[ids[:, 9]], tbl_10[ids[:, 10]], tbl_11[ids[:, 11]], tbl_12[ids[:, 12]], tbl_13[ids[:, 13]], tbl_14[ids[:, 14]], tbl_15[ids[:, 15]], tbl_16[ids[:, 16]], tbl_17[ids[:, 17]], tbl_18[ids[:, 18]], tbl_19[ids[:, 19]], tbl_20[ids[:, 20]], tbl_21[ids[:, 21]], tbl_22[ids[:, 22]], tbl_23[ids[:, 23]], tbl_24[ids[:, 24]], tbl_25[ids[:, 25]]], axis=1)
    z = _L0_rec_ref(r_dense_features, e)
    z = z.reshape(z.shape[0], -1)
    h = jnp.concatenate([z, r_dense_features], axis=1)
    h = jnp.maximum(h @ W_top1 + b_top1, 0.0)
    h = jnp.maximum(h @ W_top2 + b_top2, 0.0)
    y = h @ W_top3
    return y

_drawn_inputs = setup_inputs


def setup_inputs(seed=0):
    import zlib

    import numpy as np

    out = dict(_drawn_inputs(seed))
    spreads = {'b_top1': (0.0, 0.1), 'b_top2': (0.0, 0.1)}
    factors = {}
    for name, (base, spread) in spreads.items():
        noise = np.random.default_rng([zlib.crc32(name.encode()), seed]).standard_normal(out[name].shape)
        drawn = base * np.exp(spread * noise) if base else spread * noise
        out[name] = jnp.asarray(drawn.astype(out[name].dtype))
    for name, factor in factors.items():
        out[name] = (out[name] * factor).astype(out[name].dtype)
    return out
```

```python
from contextlib import ExitStack

import concourse.bass as bass
from concourse import mybir

F32 = mybir.dt.float32
BF16 = mybir.dt.bfloat16
I32 = mybir.dt.int32
I16 = mybir.dt.int16
ALU = mybir.AluOpType
ACT = mybir.ActivationFunctionType

P = 128
BATCH = 512
TABLES = 26
FEATURES = TABLES + 1
HOT = (12, 14, 18, 19)
HOT_ROWS = 1000
HP = 125
HC = HOT_ROWS // HP
NHOT = len(HOT)
COLD = tuple(f for f in range(TABLES) if f not in HOT)
EXTRAS = 1 + NHOT
GB = 64
GROUPS = BATCH // GB
PAIRS = GROUPS // 2
PB = 2 * GB
GATHERS = len(COLD) // 2
BANKFULS = (4, 4, 3)
NB = len(BANKFULS)
SLOT = 32
QUADRANTS = P // SLOT
COLS = 28
STEPS = COLS // QUADRANTS
KT = STEPS + 1
FOURS = GB // QUADRANTS
EARLY = (EXTRAS + 2 * BANKFULS[0]) // QUADRANTS
ALL_TILES = (0, STEPS)
EARLY_TILES, LATE_TILES = (0, EARLY), (EARLY, STEPS)
H1, H2 = 512, 256
N1 = H1 // P


def dlrm_program(nc, ids, first_row, hot_ids, row_number, hot_tables, table, dense_t, eye, w1, w1_again, w2, b2, w3, y):
    with ExitStack() as ctx:
        def sb(name, shape, dt=F32):
            return ctx.enter_context(nc.sbuf_tensor(name, shape, dt))

        def ps(name, shape):
            return ctx.enter_context(nc.psum_tensor(name, shape, F32))

        def sem(name):
            return ctx.enter_context(nc.semaphore(name))

        ids_sb = sb("ids_sb", [P, GROUPS * GATHERS], I32)
        first_sb = sb("first_sb", [P, GATHERS])
        index = [sb(f"index{s}", [P, GATHERS], I32) for s in range(2)]
        rows = [sb(f"rows{s}", [P, GATHERS, P]) for s in range(2)]
        hot_ids_sb = sb("hot_ids_sb", [HP, NHOT, BATCH], I32)
        hot_ids_16 = sb("hot_ids_16", [HP, NHOT, BATCH], I16)
        row_number_sb = sb("row_number_sb", [HP, HC])
        hot_sb = sb("hot_sb", [HP, NHOT, HC, P])
        hot_rest = sb("hot_rest", [HP, NHOT, HC, P])
        hot_part = [sb(f"hot_part{i}", [HP, NHOT, HC, P], BF16) for i in range(3)]
        onehot = sb("onehot", [HP, NHOT, HC, BATCH], BF16)
        dense_sb = sb("dense_sb", [P, BATCH])
        extras = sb("extras", [P, BATCH, EXTRAS])
        eye_sb = sb("eye_sb", [P, P])
        feats = [sb(f"feats{s}", [P, GB, COLS]) for s in range(2)]
        dots = sb("dots", [P, KT, PB])
        w1_sb = sb("w1_sb", [P, KT, H1])
        w1_again_sb = sb("w1_again_sb", [P, H1])
        w2_sb = sb("w2_sb", [P, N1, H2])
        b2_sb = sb("b2_sb", [1, H2])
        ones = sb("ones", [1, P])
        w3_sb = sb("w3_sb", [P, H2])
        h1_sb = sb("h1_sb", [P, H1])
        weighted = sb("weighted", [P, H2])
        y_sb = sb("y_sb", [P, PAIRS])

        turned = [ps(f"turned{i}", [P, 512]) for i in range(NB)]
        gram = [ps(f"gram{s}", [P, 512]) for s in range(2)]
        h1_ps = ps("h1_ps", [P, H1])
        h2_ps = ps("h2_ps", [P, 512])
        hot_ps = [ps("hot_ps", [P, BATCH]), h1_ps]

        ids_in = sem("ids_in")
        hot_ids_in = [sem(f"hot_ids_in{k}") for k in range(NHOT)]
        row_number_in = sem("row_number_in")
        hot_in = [sem(f"hot_in{k}") for k in range(NHOT)]
        eye_in = sem("eye_in")
        dense_in = sem("dense_in")
        w1_in = sem("w1_in")
        w2_in = sem("w2_in")
        constants_set = sem("constants_set")
        w1_merged = sem("w1_merged")
        index_ready = sem("index_ready")
        index_taken = sem("index_taken")
        rows_in = [[sem(f"rows_in{s}_{c}") for c in range(NB)] for s in range(2)]
        rows_used = sem("rows_used")
        hot_ids_ready = sem("hot_ids_ready")
        onehot_ready = sem("onehot_ready")
        rest_ready = sem("rest_ready")
        part_ready = [sem(f"part_ready{i}") for i in range(3)]
        hot_mm = sem("hot_mm")
        hot_placed = sem("hot_placed")
        dense_placed = sem("dense_placed")
        turned_out = [sem(f"turned_out{i}") for i in range(2)]
        extras_placed = sem("extras_placed")
        gram_ready = sem("gram_ready")
        spread_act = sem("spread_act")
        spread_dve = sem("spread_dve")
        h1_mm = sem("h1_mm")
        h1_ready = sem("h1_ready")
        h2_mm = sem("h2_mm")
        y_ready = sem("y_ready")
        y_out = sem("y_out")

        block = ctx.enter_context(nc.Block())


        @block.sync
        def _(sp):
            sp.dma_start(ids_sb[:, :], ids).then_inc(ids_in, 16)
            sp.dma_start(first_sb[:, :], first_row).then_inc(ids_in, 16)
            sp.dma_start(row_number_sb[:, :], row_number).then_inc(row_number_in, 16)
            for k in range(NHOT):
                sp.dma_start(hot_ids_sb[:, k, :], hot_ids[k].partition_broadcast(HP)).then_inc(hot_ids_in[k], 16)
                if k == 2:
                    sp.dma_start(eye_sb[:, :], eye).then_inc(eye_in, 16)
                sp.dma_start(hot_sb[:, k, :, :], hot_tables[k].rearrange("(p c) d -> p c d", c=HC)).then_inc(hot_in[k], 16)
            sp.dma_start(dense_sb[:, :], dense_t).then_inc(dense_in, 16)
            sp.dma_start(w1_again_sb[:, :], w1_again).then_inc(w1_in, 16)
            for t in range(KT):
                sp.dma_start(w1_sb[:, t, :], w1[:, t, :]).then_inc(w1_in, 16)
            sp.dma_start(w2_sb[:, :, :], w2).then_inc(w2_in, 16)
            sp.dma_start(b2_sb[:, :], b2).then_inc(w2_in, 16)
            sp.dma_start(w3_sb[:, :], w3.partition_broadcast(P)).then_inc(w2_in, 16)
            sp.wait_ge(y_ready, PAIRS)
            sp.dma_start(y, y_sb[:, :]).then_inc(y_out, 16)
            sp.wait_ge(y_out, 16)

        @block.gpsimd
        def _(pool):
            def gather(pair, s, first):
                g = pair * 2 + s
                pool.wait_ge(index_ready, g + 1)
                k = 0
                for c, n in enumerate(BANKFULS):
                    if not first:
                        pool.wait_ge(rows_used, (g - 2) * NB + c + 1)
                        pool.sem_inc(index_taken, 1)
                    elif c == 0:
                        pool.sem_inc(index_taken, 1)
                    for _ in range(n):
                        nc.gpsimd.indirect_dma_start(
                            rows[s][:, k, :], None, table,
                            bass.IndirectOffsetOnAxis(ap=index[s][:, k:k + 1], axis=0),
                        ).then_inc(rows_in[s][c], 16)
                        k += 1

            for s in range(2):
                gather(0, s, True)
            with pool.Fori(1, PAIRS) as pair:
                for s in range(2):
                    gather(pair, s, False)

        def place_turned(eng, copy, pair, r):
            s, c = r // NB, r % NB
            n = 2 * BANKFULS[c]
            f0 = EXTRAS + 2 * sum(BANKFULS[:c])
            eng.wait_ge(rows_used, pair * (2 * NB) + r + 1)
            copy(feats[s][:, :, f0:f0 + n].rearrange("p b f -> p f b"),
                 turned[c][:, 0:n * GB].rearrange("p (f b) -> p f b", b=GB)).then_inc(turned_out[r % 2], 1)

        def spread(eng, copy, done, pair, s, quadrants, tiles=ALL_TILES, turn=1):
            eng.wait_ge(gram_ready, pair * 2 + s + turn)
            t0, t1 = tiles
            for j in quadrants:
                mine = gram[s][SLOT * j:SLOT * j + FEATURES, 0:FOURS * COLS].rearrange("p (m i q) -> p m i q", i=STEPS, q=QUADRANTS)
                rows_of = min(FEATURES, QUADRANTS * t1)
                for q in range(QUADRANTS):
                    last = copy(dots[SLOT * q:SLOT * q + rows_of, t0:t1, s * GB + j:(s + 1) * GB:QUADRANTS]
                                .rearrange("p i m -> p m i"), mine[0:rows_of, :, t0:t1, q])
            last.then_inc(done, 1)

        @block.vector
        def _(dve):
            def make_index(pair, s, first):
                g = pair * 2 + s
                if not first:
                    for c in range(NB):
                        dve.wait_ge(rows_in[s][c], pair * (16 * BANKFULS[c]))
                nc.vector.tensor_tensor(index[s][:, :], ids_sb[:, bass.ds(g * GATHERS, GATHERS)], first_sb[:, :],
                                        ALU.add).then_inc(index_ready, 1)

            def make_onehot(k):
                dve.wait_ge(hot_ids_ready, k + 1)
                for c in range(HC):
                    nc.vector.tensor_scalar(onehot[:, k, c, :], hot_ids_16[:, k, :], row_number_sb[:, c:c + 1], None,
                                            ALU.is_equal).then_inc(onehot_ready, 1)

            def split_rest(k, i, whole):
                dve.wait_ge(part_ready[i], k + 1)
                out, signal = (hot_rest, rest_ready) if i == 0 else (hot_part[2], part_ready[2])
                nc.vector.tensor_tensor(out[:, k, :, :], whole[:, k, :, :], hot_part[i][:, k, :, :],
                                        ALU.subtract).then_inc(signal, 1)

            def place_extras(pair, s):
                nc.vector.tensor_copy(feats[s][:, :, 0:EXTRAS],
                                      extras[:, bass.ds(pair * PB + s * GB, GB), :]).then_inc(extras_placed, 1)

            def spread_group(pair, s, tiles=ALL_TILES, turn=1):
                if tiles[0] == 0:
                    dve.wait_ge(gram_ready, pair * 2 + s + 1)
                    nc.vector.tensor_copy(dots[:, STEPS, s * GB:(s + 1) * GB],
                                          dense_sb[:, bass.ds(pair * PB + s * GB, GB)])
                spread(dve, nc.vector.tensor_copy, spread_dve, pair, s, (2, 3), tiles, turn)

            def finish(pair):
                dve.wait_ge(h2_mm, pair + 1)
                nc.vector.scalar_tensor_tensor(out=weighted[:, :], in0=h2_ps[:, 0:H2], scalar=0.0, in1=w3_sb[:, :],
                                               op0=ALU.max, op1=ALU.mult,
                                               accum_out=y_sb[:, bass.ds(pair, 1)]).then_inc(y_ready, 1)

            dve.wait_ge(ids_in, 32)
            make_index(0, 0, True)
            make_index(0, 1, True)
            dve.wait_ge(row_number_in, 16)
            make_onehot(0)
            split_rest(0, 0, hot_sb)
            make_onehot(1)
            split_rest(0, 1, hot_rest)
            split_rest(1, 0, hot_sb)
            make_onehot(2)
            split_rest(1, 1, hot_rest)
            split_rest(2, 0, hot_sb)
            make_onehot(3)
            split_rest(2, 1, hot_rest)
            split_rest(3, 0, hot_sb)
            split_rest(3, 1, hot_rest)
            make_index(1, 0, False)
            for s in range(2):
                nc.vector.memset(feats[s][:, :, FEATURES], 0.0).then_inc(constants_set, 1)
            nc.vector.memset(dots[:, :, :], 1.0).then_inc(constants_set, 1)
            nc.vector.memset(ones[:, :], 1.0).then_inc(constants_set, 1)
            dve.wait_ge(dense_in, 16)
            nc.vector.tensor_copy(extras[:, :, 0], dense_sb[:, :]).then_inc(dense_placed, 1)
            place_turned(dve, nc.vector.tensor_copy, 0, 0)
            place_turned(dve, nc.vector.tensor_copy, 0, 2)
            dve.wait_ge(w1_in, 16 * (KT + 1))
            nc.vector.tensor_tensor(w1_sb[:, STEPS, :], w1_sb[:, STEPS, :], w1_again_sb[:, :],
                                    ALU.add).then_inc(w1_merged, 1)
            dve.wait_ge(constants_set, 4)
            dve.wait_ge(dense_placed, 1)
            dve.wait_ge(hot_placed, NHOT)
            place_extras(0, 0)
            place_extras(0, 1)
            place_turned(dve, nc.vector.tensor_copy, 0, 4)
            spread_group(0, 0)
            make_index(1, 1, False)
            spread_group(0, 1)
            dve.wait_ge(w2_in, 48)

            with dve.Fori(1, PAIRS - 1) as pair:
                place_extras(pair, 0)
                place_turned(dve, nc.vector.tensor_copy, pair, 0)
                make_index(pair + 1, 0, False)
                place_turned(dve, nc.vector.tensor_copy, pair, 2)
                spread_group(pair, 0)
                place_extras(pair, 1)
                place_turned(dve, nc.vector.tensor_copy, pair, 4)
                make_index(pair + 1, 1, False)
                spread_group(pair, 1)
                finish(pair - 1)
            last = PAIRS - 1
            place_extras(last, 0)
            place_turned(dve, nc.vector.tensor_copy, last, 0)
            place_turned(dve, nc.vector.tensor_copy, last, 2)
            spread_group(last, 0)
            place_extras(last, 1)
            finish(last - 1)
            spread_group(last, 1, EARLY_TILES)
            place_turned(dve, nc.vector.tensor_copy, last, 4)
            spread_group(last, 1, LATE_TILES, 2)
            finish(last)

        @block.scalar
        def _(act):
            def split_part(k, i, whole):
                if i == 0:
                    act.wait_ge(hot_in[k], 16)
                else:
                    act.wait_ge(rest_ready, k + 1)
                nc.scalar.copy(hot_part[i][:, k, :, :], whole[:, k, :, :]).then_inc(part_ready[i], 1)

            def place_hot(k):
                act.wait_ge(hot_mm, k + 1)
                nc.scalar.copy(extras[:, :, 1 + k], hot_ps[k % 2][:, :]).then_inc(hot_placed, 1)

            def relu_h1(pair):
                act.wait_ge(h1_mm, pair + 1)
                nc.scalar.activation(h1_sb[:, :], h1_ps[:, :], ACT.Relu).then_inc(h1_ready, 1)

            def cast_ids(k):
                act.wait_ge(hot_ids_in[k], 16)
                nc.scalar.copy(hot_ids_16[:, k, :], hot_ids_sb[:, k, :]).then_inc(hot_ids_ready, 1)

            cast_ids(0)
            split_part(0, 0, hot_sb)
            cast_ids(1)
            split_part(1, 0, hot_sb)
            split_part(0, 1, hot_rest)
            cast_ids(2)
            split_part(2, 0, hot_sb)
            split_part(1, 1, hot_rest)
            cast_ids(3)
            split_part(3, 0, hot_sb)
            place_hot(0)
            split_part(2, 1, hot_rest)
            split_part(3, 1, hot_rest)
            place_hot(1)
            place_hot(2)
            place_turned(act, nc.scalar.copy, 0, 1)
            place_hot(3)
            place_turned(act, nc.scalar.copy, 0, 3)
            place_turned(act, nc.scalar.copy, 0, 5)
            act.wait_ge(constants_set, 4)
            for s in range(2):
                spread(act, nc.scalar.copy, spread_act, 0, s, (0, 1))
            def turned_and_spread(pair, tail):
                place_turned(act, nc.scalar.copy, pair, 1)
                relu_h1(pair - 1)
                spread(act, nc.scalar.copy, spread_act, pair, 0, (0, 1))
                place_turned(act, nc.scalar.copy, pair, 3)
                if tail:
                    spread(act, nc.scalar.copy, spread_act, pair, 1, (0, 1), EARLY_TILES)
                place_turned(act, nc.scalar.copy, pair, 5)
                spread(act, nc.scalar.copy, spread_act, pair, 1, (0, 1), *((LATE_TILES, 2) if tail else ()))

            with act.Fori(1, PAIRS - 1) as pair:
                turned_and_spread(pair, False)
            turned_and_spread(PAIRS - 1, True)
            relu_h1(PAIRS - 1)

        @block.tensor
        def _(pe):
            def hot_lookup(k):
                if k >= 2:
                    pe.wait_ge(hot_placed, k - 1)
                for i in range(3):
                    pe.wait_ge(part_ready[i], k + 1)
                    for c in range(HC):
                        if i == 0:
                            pe.wait_ge(onehot_ready, HC * k + c + 1)
                        last = nc.tensor.matmul(hot_ps[k % 2][:, :], hot_part[i][:, k, c, :], onehot[:, k, c, :],
                                                start=i == 0 and c == 0, stop=i == 2 and c == HC - 1)
                last.then_inc(hot_mm, 1)

            def turn(pair, r, first):
                s, c = r // NB, r % NB
                pe.wait_ge(rows_in[s][c], (pair + 1) * (16 * BANKFULS[c]))
                if r >= NB:
                    pe.wait_ge(turned_out[(r - NB) % 2], pair * NB + (r - NB) // 2 + 1)
                elif not first:
                    pe.wait_ge(turned_out[(r + NB) % 2], (pair - 1) * NB + (r + NB) // 2 + 1)
                for i in range(BANKFULS[c]):
                    last = nc.tensor.transpose(turned[c][:, i * P:(i + 1) * P],
                                               rows[s][:, sum(BANKFULS[:c]) + i, :], eye_sb[:, :])
                last.then_inc(rows_used, 1)

            def form_dots(pair, s, tiles=ALL_TILES):
                pe.wait_ge(extras_placed, pair * 2 + s + 1)
                if tiles == EARLY_TILES:
                    pe.wait_ge(turned_out[1], pair * NB + 2)
                else:
                    pe.wait_ge(turned_out[0], pair * NB + 2 + s)
                    pe.wait_ge(turned_out[1], pair * NB + 1 + 2 * s)
                if tiles == LATE_TILES:
                    pe.wait_ge(spread_dve, pair * 2 + 2)
                    pe.wait_ge(spread_act, pair * 2 + 2)
                v0, v1 = (QUADRANTS * t for t in tiles)
                u1 = min(FEATURES, v1)
                for m in range(FOURS):
                    for j in range(QUADRANTS):
                        b = QUADRANTS * m + j
                        last = nc.tensor.matmul(gram[s][SLOT * j:SLOT * j + u1, m * COLS + v0:m * COLS + v1],
                                                feats[s][:, b, 0:u1], feats[s][:, b, v0:v1], start=True, stop=True)
                last.then_inc(gram_ready, 1)

            def layer1(pair, tiles, spreads=0):
                if spreads:
                    pe.wait_ge(spread_dve, pair * 2 + spreads)
                    pe.wait_ge(spread_act, pair * 2 + spreads)
                for t in tiles:
                    for n in range(N1):
                        last = nc.tensor.matmul(h1_ps[:, n * PB:(n + 1) * PB], w1_sb[:, t, n * P:(n + 1) * P], dots[:, t, :],
                                                start=t == STEPS and n == 0, stop=t == STEPS - 1, skip_group_check=True)
                if tiles[-1] == STEPS - 1:
                    last.then_inc(h1_mm, 1)

            def bias2(pair):
                if isinstance(pair, int) and pair:
                    pe.wait_ge(y_ready, pair)
                nc.tensor.matmul(h2_ps[:, 0:H2], ones[:, :], b2_sb[:, :], start=True, stop=False)

            def layer2(pair, chunks):
                if chunks[0] == 0:
                    pe.wait_ge(h1_ready, pair + 1)
                for n in chunks:
                    last = nc.tensor.matmul(h2_ps[:, 0:H2], h1_sb[:, n * PB:(n + 1) * PB], w2_sb[:, n, :],
                                            start=False, stop=n == N1 - 1)
                if chunks[-1] == N1 - 1:
                    last.then_inc(h2_mm, 1)

            for k in range(3):
                hot_lookup(k)
            pe.wait_ge(eye_in, 16)
            for r in range(NB):
                turn(0, r, True)
            hot_lookup(3)
            for r in range(NB, 2 * NB):
                turn(0, r, True)
            pe.wait_ge(constants_set, 4)
            form_dots(0, 0)
            form_dots(0, 1)
            pe.wait_ge(w1_merged, 1)
            pe.wait_ge(w2_in, 48)
            def first_half(pair):
                turn(pair, 0, False)
                layer1(pair - 1, (STEPS, 0, 1, 2), spreads=2)
                turn(pair, 1, False)
                layer1(pair - 1, (3, 4, 5))
                turn(pair, 2, False)
                layer1(pair - 1, (6,))
                form_dots(pair, 0)
                turn(pair, 3, False)

            with pe.Fori(1, PAIRS - 1) as pair:
                first_half(pair)
                turn(pair, 4, False)
                turn(pair, 5, False)
                bias2(pair - 1)
                layer2(pair - 1, (0,))
                form_dots(pair, 1)
                layer2(pair - 1, (1, 2, 3))
            last = PAIRS - 1
            first_half(last)
            bias2(last - 1)
            layer2(last - 1, range(N1))
            form_dots(last, 1, EARLY_TILES)
            turn(last, 4, False)
            layer1(last, (STEPS,) + tuple(range(*EARLY_TILES)), spreads=2)
            turn(last, 5, False)
            form_dots(last, 1, LATE_TILES)
            layer1(last, range(*LATE_TILES), spreads=3)
            bias2(last)
            layer2(last, range(N1))


def kernel(**inputs):
    import numpy as np
    import concourse.bacc as bacc
    from concourse.bass_utils import run_bass_kernel_spmd

    a = {k: np.asarray(v) for k, v in inputs.items()}
    cold = [a[f"tbl_{f}"] for f in COLD]
    starts = np.cumsum([0] + [len(t) for t in cold[:-1]]).astype(np.float32)

    ids = a["ids"][:, COLD].reshape(GROUPS, GB, GATHERS, 2).transpose(3, 1, 0, 2).reshape(P, GROUPS * GATHERS)
    first_row = np.repeat(starts.reshape(GATHERS, 2).T, GB, axis=0)
    row_number = np.arange(HOT_ROWS, dtype=np.float32).reshape(HP, HC)

    slot = {0: 0}
    slot.update({1 + f: n for n, f in enumerate(HOT + COLD, 1)})
    w = a["W_top1"]
    w1 = np.zeros((P, KT, H1), np.float32)
    pair_row = P
    for f in range(FEATURES):
        for g in range(f + 1, FEATURES):
            u, v = sorted((slot[f], slot[g]))
            w1[SLOT * (v % QUADRANTS) + u, v // QUADRANTS] = w[pair_row]
            pair_row += 1
    w1[FEATURES, 0] = a["b_top1"]
    w1[:, STEPS] = w[0:P]
    arrays = {
        "ids": ids, "first_row": first_row, "hot_ids": a["ids"][:, HOT].T, "row_number": row_number,
        "hot_tables": np.stack([a[f"tbl_{f}"] for f in HOT]), "table": np.concatenate(cold, axis=0),
        "dense_t": a["r_dense_features"].T, "eye": np.eye(P, dtype=np.float32),
        "w1": w1, "w1_again": w[pair_row:pair_row + P],
        "w2": a["W_top2"].reshape(N1, P, H2).transpose(1, 0, 2),
        "b2": a["b_top2"].reshape(1, H2), "w3": a["W_top3"].reshape(H2),
    }
    arrays = {k: np.ascontiguousarray(v) for k, v in arrays.items()}
    nc = bacc.Bacc("TRN2", target_bir_lowering=False, num_devices=1)
    args = [nc.dram_tensor(k, v.shape, mybir.dt.from_np(v.dtype), kind="ExternalInput").ap() for k, v in arrays.items()]
    y = nc.dram_tensor("y", (P, PAIRS), F32, kind="ExternalOutput").ap()
    dlrm_program(nc, *args, y)
    result = run_bass_kernel_spmd(nc, [arrays], core_ids=[0])
    return result.results[0]["y"].T.reshape(BATCH, 1)
```

```python
from contextlib import ExitStack

import concourse.bass as bass
from concourse import mybir

F32 = mybir.dt.float32
BF16 = mybir.dt.bfloat16
I32 = mybir.dt.int32
I16 = mybir.dt.int16
ALU = mybir.AluOpType
ACT = mybir.ActivationFunctionType

P = 128
BATCH = 512
TABLES = 26
FEATURES = TABLES + 1
HOT = (12, 14, 18, 19)
HOT_ROWS = 1000
HP = 125
HC = HOT_ROWS // HP
NHOT = len(HOT)
COLD = tuple(f for f in range(TABLES) if f not in HOT)
EXTRAS = 1 + NHOT
GB = 64
GROUPS = BATCH // GB
PAIRS = GROUPS // 2
PB = 2 * GB
GATHERS = len(COLD) // 2
BANKFULS = (4, 4, 3)
NB = len(BANKFULS)
SLOT = 32
QUADRANTS = P // SLOT
COLS = 28
STEPS = COLS // QUADRANTS
KT = STEPS + 1
FOURS = GB // QUADRANTS
ALL_TILES = (0, STEPS)
CUT_BANKS = (1, NB)
NCUTS = len(CUT_BANKS)
CUTS = [0] + [(EXTRAS + 2 * sum(BANKFULS[:c])) // QUADRANTS for c in CUT_BANKS[:-1]] + [STEPS]
CUT_TILES = [(CUTS[c], CUTS[c + 1]) for c in range(NCUTS)]
H1, H2 = 512, 256
N1 = H1 // P


def dlrm_program(nc, ids, first_row, hot_ids, row_number, hot_tables, table, dense_t, eye, w1, w1_again, w2, b2, w3, y):
    with ExitStack() as ctx:
        def sb(name, shape, dt=F32):
            return ctx.enter_context(nc.sbuf_tensor(name, shape, dt))

        def ps(name, shape):
            return ctx.enter_context(nc.psum_tensor(name, shape, F32))

        def sem(name):
            return ctx.enter_context(nc.semaphore(name))

        ids_sb = sb("ids_sb", [P, GROUPS * GATHERS], I32)
        first_sb = sb("first_sb", [P, GATHERS])
        index = [sb(f"index{s}", [P, GATHERS], I32) for s in range(2)]
        rows = [sb(f"rows{s}", [P, GATHERS, P]) for s in range(2)]
        hot_ids_sb = sb("hot_ids_sb", [HP, NHOT * BATCH], I32)
        hot_ids_16 = sb("hot_ids_16", [HP, NHOT * BATCH], I16)
        row_number_sb = sb("row_number_sb", [HP, HC])
        hot_sb = sb("hot_sb", [HP, NHOT, HC, P])
        hot_rest = sb("hot_rest", [HP, NHOT, HC, P])
        hot_part = [sb(f"hot_part{i}", [HP, NHOT, HC, P], BF16) for i in range(3)]
        onehot = sb("onehot", [HP, HC, NHOT * PB], BF16)
        dense_sb = sb("dense_sb", [P, BATCH])
        eye_sb = sb("eye_sb", [P, P])
        feats = [sb(f"feats{s}", [P, GB, COLS]) for s in range(2)]
        dots = sb("dots", [P, KT, PB])
        w1_sb = sb("w1_sb", [P, KT, H1])
        w1_again_sb = sb("w1_again_sb", [P, H1])
        w2_sb = sb("w2_sb", [P, N1, H2])
        b2_sb = sb("b2_sb", [1, H2])
        ones = sb("ones", [1, P])
        w3_sb = sb("w3_sb", [P, H2])
        h1_sb = sb("h1_sb", [P, H1])
        weighted = sb("weighted", [P, H2])
        y_sb = sb("y_sb", [P, PAIRS])

        turned = [ps(f"turned{i}", [P, 512]) for i in range(NB)]
        gram = [ps(f"gram{s}", [P, 512]) for s in range(2)]
        h1_ps = ps("h1_ps", [P, H1])
        h2_ps = ps("h2_ps", [P, 512])
        hot_ps = ps("hot_ps", [P, NHOT, PB])

        ids_in = sem("ids_in")
        hot_ids_in = [sem(f"hot_ids_in{i}") for i in range(3)]
        row_number_in = sem("row_number_in")
        hot_in = [sem(f"hot_in{k}") for k in range(NHOT)]
        eye_in = sem("eye_in")
        dense_in = sem("dense_in")
        w1_dense_in = sem("w1_dense_in")
        w1_in = sem("w1_in")
        w2_in = sem("w2_in")
        constants_set = sem("constants_set")
        w1_merged = sem("w1_merged")
        index_ready = sem("index_ready")
        index_taken = sem("index_taken")
        rows_in = [[sem(f"rows_in{s}_{c}") for c in range(NB)] for s in range(2)]
        rows_used = sem("rows_used")
        hot_ids_ready = sem("hot_ids_ready")
        onehot_ready = sem("onehot_ready")
        rest_ready = sem("rest_ready")
        part_ready = [sem(f"part_ready{i}") for i in range(3)]
        hot_mm = sem("hot_mm")
        turned_out = [sem(f"turned_out{i}") for i in range(2)]
        extras_placed = sem("extras_placed")
        gram_ready = sem("gram_ready")
        spread_act = sem("spread_act")
        spread_dve = sem("spread_dve")
        h1_mm = sem("h1_mm")
        h1_ready = sem("h1_ready")
        h2_mm = sem("h2_mm")
        y_ready = sem("y_ready")
        y_out = sem("y_out")

        block = ctx.enter_context(nc.Block())


        @block.sync
        def _(sp):
            sp.dma_start(ids_sb[:, :], ids).then_inc(ids_in, 16)
            sp.dma_start(row_number_sb[:, :], row_number).then_inc(row_number_in, 16)
            one_pair = NHOT * PB
            sp.dma_start(hot_ids_sb[:, 0:one_pair], hot_ids[0:one_pair].partition_broadcast(HP)).then_inc(hot_ids_in[0], 16)
            for k in range(NHOT):
                sp.dma_start(hot_sb[:, k, :, :], hot_tables[k].rearrange("(p c) d -> p c d", c=HC)).then_inc(hot_in[k], 16)
            sp.dma_start(eye_sb[:, :], eye).then_inc(eye_in, 16)
            sp.dma_start(dense_sb[:, :], dense_t).then_inc(dense_in, 16)
            sp.wait_ge(rows_in[0][0], 16 * BANKFULS[0])
            sp.dma_start(hot_ids_sb[:, one_pair:2 * one_pair],
                         hot_ids[one_pair:2 * one_pair].partition_broadcast(HP)).then_inc(hot_ids_in[1], 16)
            sp.wait_ge(rows_in[0][1], 16 * BANKFULS[1])
            sp.dma_start(w1_again_sb[:, :], w1_again).then_inc(w1_dense_in, 16)
            sp.dma_start(w1_sb[:, STEPS, :], w1[:, STEPS, :]).then_inc(w1_dense_in, 16)
            sp.dma_start(w1_sb[:, 0, :], w1[:, 0, :]).then_inc(w1_in, 16)
            sp.wait_ge(rows_in[0][2], 16 * BANKFULS[2])
            for t in (1, 2, 3):
                sp.dma_start(w1_sb[:, t, :], w1[:, t, :]).then_inc(w1_in, 16)
            sp.wait_ge(rows_in[1][0], 16 * BANKFULS[0])
            for t in (4, 5, 6):
                sp.dma_start(w1_sb[:, t, :], w1[:, t, :]).then_inc(w1_in, 16)
            sp.wait_ge(rows_in[1][1], 16 * BANKFULS[1])
            sp.dma_start(hot_ids_sb[:, 2 * one_pair:],
                         hot_ids[2 * one_pair:].partition_broadcast(HP)).then_inc(hot_ids_in[2], 16)
            sp.dma_start(w2_sb[:, :, :], w2).then_inc(w2_in, 16)
            sp.dma_start(b2_sb[:, :], b2).then_inc(w2_in, 16)
            sp.dma_start(w3_sb[:, :], w3.partition_broadcast(P)).then_inc(w2_in, 16)
            sp.wait_ge(y_ready, PAIRS)
            sp.dma_start(y, y_sb[:, :]).then_inc(y_out, 16)
            sp.wait_ge(y_out, 16)

        @block.gpsimd
        def _(pool):
            def gather(pair, s, first):
                g = pair * 2 + s
                pool.wait_ge(index_ready, g + 1)
                k = 0
                for c, n in enumerate(BANKFULS):
                    if not first:
                        pool.wait_ge(rows_used, (g - 2) * NB + c + 1)
                        pool.sem_inc(index_taken, 1)
                    elif c == 0:
                        pool.sem_inc(index_taken, 1)
                    for _ in range(n):
                        nc.gpsimd.indirect_dma_start(
                            rows[s][:, k, :], None, table,
                            bass.IndirectOffsetOnAxis(ap=index[s][:, k:k + 1], axis=0),
                        ).then_inc(rows_in[s][c], 16)
                        k += 1

            for s in range(2):
                gather(0, s, True)
            with pool.Fori(1, PAIRS) as pair:
                for s in range(2):
                    gather(pair, s, False)

        def place_turned(eng, copy, pair, r):
            s, c = r // NB, r % NB
            n = 2 * BANKFULS[c]
            f0 = EXTRAS + 2 * sum(BANKFULS[:c])
            eng.wait_ge(rows_used, pair * (2 * NB) + r + 1)
            copy(feats[s][:, :, f0:f0 + n].rearrange("p b f -> p f b"),
                 turned[c][:, 0:n * GB].rearrange("p (f b) -> p f b", b=GB)).then_inc(turned_out[r % 2], 1)

        def spread(eng, copy, done, pair, s, quadrants, tiles=ALL_TILES, turn=1):
            eng.wait_ge(gram_ready, pair * 2 + s + turn)
            if done is spread_dve and tiles[0] == 0:
                nc.vector.tensor_copy(dots[:, STEPS, s * GB:(s + 1) * GB],
                                      feats[s][:, :, 0])
            t0, t1 = tiles
            for j in quadrants:
                mine = gram[s][SLOT * j:SLOT * j + FEATURES, 0:FOURS * COLS].rearrange("p (m i q) -> p m i q", i=STEPS, q=QUADRANTS)
                rows_of = min(FEATURES, QUADRANTS * t1)
                for q in range(QUADRANTS):
                    last = copy(dots[SLOT * q:SLOT * q + rows_of, t0:t1, s * GB + j:(s + 1) * GB:QUADRANTS]
                                .rearrange("p i m -> p m i"), mine[0:rows_of, :, t0:t1, q])
            last.then_inc(done, 1)

        @block.vector
        def _(dve):
            def make_index(pair, s, first):
                g = pair * 2 + s
                if not first:
                    for c in range(NB):
                        dve.wait_ge(rows_in[s][c], pair * (16 * BANKFULS[c]))
                nc.vector.tensor_tensor(index[s][:, :], ids_sb[:, bass.ds(g * GATHERS, GATHERS)], first_sb[:, :],
                                        ALU.add).then_inc(index_ready, 1)

            def make_onehot(pair):
                dve.wait_ge(hot_ids_ready, pair + 1 if isinstance(pair, int) else 3)
                for c in range(HC):
                    nc.vector.tensor_scalar(onehot[:, c, :], hot_ids_16[:, bass.ds(pair * (NHOT * PB), NHOT * PB)],
                                            row_number_sb[:, c:c + 1], None, ALU.is_equal).then_inc(onehot_ready, 1)

            def split_rest(k, i, whole):
                dve.wait_ge(part_ready[i], k + 1)
                out, signal = (hot_rest, rest_ready) if i == 0 else (hot_part[2], part_ready[2])
                nc.vector.tensor_tensor(out[:, k, :, :], whole[:, k, :, :], hot_part[i][:, k, :, :],
                                        ALU.subtract).then_inc(signal, 1)

            def place_extras(pair, first=False):
                if not first:
                    dve.wait_ge(spread_dve, pair * 2)
                dve.wait_ge(hot_mm, pair + 1)
                for s in range(2):
                    nc.vector.tensor_copy(feats[s][:, :, 1:EXTRAS].rearrange("p b k -> p k b"),
                                          hot_ps[:, :, s * GB:(s + 1) * GB])
                    nc.vector.tensor_copy(feats[s][:, :, 0],
                                          dense_sb[:, bass.ds(pair * PB + s * GB, GB)]).then_inc(extras_placed, 1)

            def spread_group(pair, s, tiles=ALL_TILES, turn=1):
                spread(dve, nc.vector.tensor_copy, spread_dve, pair, s, (2, 3), tiles, turn)

            def finish(pair):
                dve.wait_ge(h2_mm, pair + 1)
                nc.vector.scalar_tensor_tensor(out=weighted[:, :], in0=h2_ps[:, 0:H2], scalar=0.0, in1=w3_sb[:, :],
                                               op0=ALU.max, op1=ALU.mult,
                                               accum_out=y_sb[:, bass.ds(pair, 1)]).then_inc(y_ready, 1)

            dve.wait_ge(ids_in, 32)
            make_index(0, 0, True)
            make_index(0, 1, True)
            for s in range(2):
                nc.vector.memset(feats[s][:, :, FEATURES], 0.0).then_inc(constants_set, 1)
            nc.vector.memset(dots[:, :, :], 1.0).then_inc(constants_set, 1)
            nc.vector.memset(ones[:, :], 1.0).then_inc(constants_set, 1)
            dve.wait_ge(row_number_in, 16)
            make_onehot(0)
            split_rest(0, 0, hot_sb)
            for k in range(1, NHOT):
                split_rest(k, 0, hot_sb)
                split_rest(k - 1, 1, hot_rest)
            split_rest(NHOT - 1, 1, hot_rest)
            place_turned(dve, nc.vector.tensor_copy, 0, 0)
            dve.wait_ge(dense_in, 16)
            place_extras(0, True)
            place_turned(dve, nc.vector.tensor_copy, 0, 2)
            make_onehot(1)
            make_index(1, 0, False)
            dve.wait_ge(constants_set, 4)
            spread_group(0, 0)
            dve.wait_ge(w1_dense_in, 32)
            nc.vector.tensor_tensor(w1_sb[:, STEPS, :], w1_sb[:, STEPS, :], w1_again_sb[:, :],
                                    ALU.add).then_inc(w1_merged, 1)
            place_turned(dve, nc.vector.tensor_copy, 0, 4)
            make_index(1, 1, False)
            spread_group(0, 1)
            dve.wait_ge(w2_in, 48)

            with dve.Fori(1, PAIRS - 1) as pair:
                place_extras(pair)
                place_turned(dve, nc.vector.tensor_copy, pair, 0)
                make_onehot(pair + 1)
                make_index(pair + 1, 0, False)
                place_turned(dve, nc.vector.tensor_copy, pair, 2)
                spread_group(pair, 0)
                place_turned(dve, nc.vector.tensor_copy, pair, 4)
                make_index(pair + 1, 1, False)
                finish(pair - 1)
                spread_group(pair, 1)
            last = PAIRS - 1
            place_extras(last)
            place_turned(dve, nc.vector.tensor_copy, last, 0)
            place_turned(dve, nc.vector.tensor_copy, last, 2)
            spread_group(last, 0)
            spread_group(last, 1, CUT_TILES[0])
            place_turned(dve, nc.vector.tensor_copy, last, 4)
            for c in range(1, NCUTS):
                spread_group(last, 1, CUT_TILES[c], 1 + c)
            finish(last - 1)
            finish(last)

        @block.scalar
        def _(act):
            def split_part(k, i, whole):
                if i == 0:
                    act.wait_ge(hot_in[k], 16)
                else:
                    act.wait_ge(rest_ready, k + 1)
                nc.scalar.copy(hot_part[i][:, k, :, :], whole[:, k, :, :]).then_inc(part_ready[i], 1)

            def relu_h1(pair):
                act.wait_ge(h1_mm, pair + 1)
                nc.scalar.activation(h1_sb[:, :], h1_ps[:, :], ACT.Relu).then_inc(h1_ready, 1)

            def cast_ids(i, ids_of):
                act.wait_ge(hot_ids_in[i], 16)
                nc.scalar.copy(hot_ids_16[:, ids_of], hot_ids_sb[:, ids_of]).then_inc(hot_ids_ready, 1)

            act.dma_start(first_sb[:, :], first_row).then_inc(ids_in, 16)
            cast_ids(0, slice(0, NHOT * PB))
            split_part(0, 0, hot_sb)
            for k in range(1, NHOT):
                split_part(k, 0, hot_sb)
                split_part(k - 1, 1, hot_rest)
            split_part(NHOT - 1, 1, hot_rest)
            place_turned(act, nc.scalar.copy, 0, 1)
            cast_ids(1, slice(NHOT * PB, 2 * NHOT * PB))
            place_turned(act, nc.scalar.copy, 0, 3)
            act.wait_ge(constants_set, 4)
            spread(act, nc.scalar.copy, spread_act, 0, 0, (0, 1))
            place_turned(act, nc.scalar.copy, 0, 5)
            spread(act, nc.scalar.copy, spread_act, 0, 1, (0, 1))
            cast_ids(2, slice(2 * NHOT * PB, NHOT * BATCH))

            def turned_and_spread(pair, tail):
                place_turned(act, nc.scalar.copy, pair, 1)
                relu_h1(pair - 1)
                spread(act, nc.scalar.copy, spread_act, pair, 0, (0, 1))
                place_turned(act, nc.scalar.copy, pair, 3)
                if tail:
                    for c in range(NCUTS - 1):
                        spread(act, nc.scalar.copy, spread_act, pair, 1, (0, 1), CUT_TILES[c], 1 + c)
                place_turned(act, nc.scalar.copy, pair, 5)
                spread(act, nc.scalar.copy, spread_act, pair, 1, (0, 1), *((CUT_TILES[-1], NCUTS) if tail else ()))

            with act.Fori(1, PAIRS - 1) as pair:
                turned_and_spread(pair, False)
            turned_and_spread(PAIRS - 1, True)
            relu_h1(PAIRS - 1)

        @block.tensor
        def _(pe):
            def hot_lookup(pair, tables):
                if tables[0] == 0:
                    pe.wait_ge(onehot_ready, HC * (pair + 1))
                for k in tables:
                    for i in range(3):
                        pe.wait_ge(part_ready[i], k + 1)
                        for c in range(HC):
                            last = nc.tensor.matmul(hot_ps[:, k, :], hot_part[i][:, k, c, :],
                                                    onehot[:, c, k * PB:(k + 1) * PB],
                                                    start=i == 0 and c == 0, stop=i == 2 and c == HC - 1)
                if tables[-1] == NHOT - 1:
                    last.then_inc(hot_mm, 1)

            def turn(pair, r, first):
                s, c = r // NB, r % NB
                pe.wait_ge(rows_in[s][c], (pair + 1) * (16 * BANKFULS[c]))
                if r >= NB:
                    pe.wait_ge(turned_out[(r - NB) % 2], pair * NB + (r - NB) // 2 + 1)
                elif not first:
                    pe.wait_ge(turned_out[(r + NB) % 2], (pair - 1) * NB + (r + NB) // 2 + 1)
                for i in range(BANKFULS[c]):
                    last = nc.tensor.transpose(turned[c][:, i * P:(i + 1) * P],
                                               rows[s][:, sum(BANKFULS[:c]) + i, :], eye_sb[:, :])
                last.then_inc(rows_used, 1)

            def form_dots(pair, s, tiles=ALL_TILES):
                pe.wait_ge(extras_placed, pair * 2 + s + 1)
                r = s * NB + (NB if tiles == ALL_TILES else CUT_BANKS[CUT_TILES.index(tiles)]) - 1
                for i in range(2):
                    pe.wait_ge(turned_out[i], pair * NB + (r - i) // 2 + 1)
                if tiles != ALL_TILES and tiles[0] > 0:
                    pe.wait_ge(spread_dve, pair * 2 + 1 + CUT_TILES.index(tiles))
                    pe.wait_ge(spread_act, pair * 2 + 1 + CUT_TILES.index(tiles))
                v0, v1 = (QUADRANTS * t for t in tiles)
                u1 = min(FEATURES, v1)
                for m in range(FOURS):
                    for j in range(QUADRANTS):
                        b = QUADRANTS * m + j
                        last = nc.tensor.matmul(gram[s][SLOT * j:SLOT * j + u1, m * COLS + v0:m * COLS + v1],
                                                feats[s][:, b, 0:u1], feats[s][:, b, v0:v1], start=True, stop=True)
                last.then_inc(gram_ready, 1)

            def layer1(pair, tiles, spreads=0):
                if spreads:
                    pe.wait_ge(spread_dve, pair * 2 + spreads)
                    pe.wait_ge(spread_act, pair * 2 + spreads)
                for t in tiles:
                    for n in range(N1):
                        last = nc.tensor.matmul(h1_ps[:, n * PB:(n + 1) * PB], w1_sb[:, t, n * P:(n + 1) * P], dots[:, t, :],
                                                start=t == STEPS and n == 0, stop=t == STEPS - 1, skip_group_check=True)
                if tiles[-1] == STEPS - 1:
                    last.then_inc(h1_mm, 1)

            def bias2(pair):
                if isinstance(pair, int) and pair:
                    pe.wait_ge(y_ready, pair)
                nc.tensor.matmul(h2_ps[:, 0:H2], ones[:, :], b2_sb[:, :], start=True, stop=False)

            def layer2(pair, chunks):
                if chunks[0] == 0:
                    pe.wait_ge(h1_ready, pair + 1)
                for n in chunks:
                    last = nc.tensor.matmul(h2_ps[:, 0:H2], h1_sb[:, n * PB:(n + 1) * PB], w2_sb[:, n, :],
                                            start=False, stop=n == N1 - 1)
                if chunks[-1] == N1 - 1:
                    last.then_inc(h2_mm, 1)

            hot_lookup(0, range(NHOT - 1))
            pe.wait_ge(eye_in, 16)
            turn(0, 0, True)
            turn(0, 1, True)
            hot_lookup(0, (NHOT - 1,))
            turn(0, 2, True)
            pe.wait_ge(constants_set, 4)
            form_dots(0, 0)
            turn(0, 3, True)
            hot_lookup(1, (0, 1))
            turn(0, 4, True)
            hot_lookup(1, (2,))
            turn(0, 5, True)
            form_dots(0, 1)
            pe.wait_ge(w1_merged, 1)
            pe.wait_ge(w1_in, 16 * STEPS)
            pe.wait_ge(w2_in, 48)

            def first_half(pair):
                hot_lookup(pair, (3,))
                turn(pair, 0, False)
                layer1(pair - 1, (STEPS, 0, 1, 2), spreads=2)
                turn(pair, 1, False)
                layer1(pair - 1, (3, 4, 5))
                turn(pair, 2, False)
                layer1(pair - 1, (6,))
                form_dots(pair, 0)
                turn(pair, 3, False)
                bias2(pair - 1)

            with pe.Fori(1, PAIRS - 1) as pair:
                first_half(pair)
                layer2(pair - 1, (0, 1))
                hot_lookup(pair + 1, (0,))
                turn(pair, 4, False)
                layer2(pair - 1, (2, 3))
                hot_lookup(pair + 1, (1,))
                turn(pair, 5, False)
                hot_lookup(pair + 1, (2,))
                form_dots(pair, 1)
            last = PAIRS - 1
            first_half(last)
            layer2(last - 1, (0,1,))
            form_dots(last, 1, CUT_TILES[0])
            layer2(last - 1, (2,3,))
            turn(last, 4, False)
            layer1(last, (STEPS, 0,), spreads=2)
            turn(last, 5, False)
            layer1(last, (1,))
            form_dots(last, 1, CUT_TILES[1])
            layer1(last, (2,))
            layer1(last, (3, 4, 5, 6,), spreads=3)
            bias2(last)
            layer2(last, range(N1))


def kernel(**inputs):
    import numpy as np
    import concourse.bacc as bacc
    from concourse.bass_utils import run_bass_kernel_spmd

    a = {k: np.asarray(v) for k, v in inputs.items()}
    cold = [a[f"tbl_{f}"] for f in COLD]
    starts = np.cumsum([0] + [len(t) for t in cold[:-1]]).astype(np.float32)

    ids = a["ids"][:, COLD].reshape(GROUPS, GB, GATHERS, 2).transpose(3, 1, 0, 2).reshape(P, GROUPS * GATHERS)
    first_row = np.repeat(starts.reshape(GATHERS, 2).T, GB, axis=0)
    hot_ids = a["ids"][:, HOT].reshape(PAIRS, PB, NHOT).transpose(0, 2, 1).reshape(-1)
    row_number = np.arange(HOT_ROWS, dtype=np.float32).reshape(HP, HC)

    slot = {0: 0}
    slot.update({1 + f: n for n, f in enumerate(HOT + COLD, 1)})
    w = a["W_top1"]
    w1 = np.zeros((P, KT, H1), np.float32)
    pair_row = P
    for f in range(FEATURES):
        for g in range(f + 1, FEATURES):
            u, v = sorted((slot[f], slot[g]))
            w1[SLOT * (v % QUADRANTS) + u, v // QUADRANTS] = w[pair_row]
            pair_row += 1
    w1[FEATURES, 0] = a["b_top1"]
    w1[:, STEPS] = w[0:P]
    arrays = {
        "ids": ids, "first_row": first_row, "hot_ids": hot_ids, "row_number": row_number,
        "hot_tables": np.stack([a[f"tbl_{f}"] for f in HOT]), "table": np.concatenate(cold, axis=0),
        "dense_t": a["r_dense_features"].T, "eye": np.eye(P, dtype=np.float32),
        "w1": w1, "w1_again": w[pair_row:pair_row + P],
        "w2": a["W_top2"].reshape(N1, P, H2).transpose(1, 0, 2),
        "b2": a["b_top2"].reshape(1, H2), "w3": a["W_top3"].reshape(H2),
    }
    arrays = {k: np.ascontiguousarray(v) for k, v in arrays.items()}
    nc = bacc.Bacc("TRN2", target_bir_lowering=False, num_devices=1)
    args = [nc.dram_tensor(k, v.shape, mybir.dt.from_np(v.dtype), kind="ExternalInput").ap() for k, v in arrays.items()]
    y = nc.dram_tensor("y", (P, PAIRS), F32, kind="ExternalOutput").ap()
    dlrm_program(nc, *args, y)
    result = run_bass_kernel_spmd(nc, [arrays], core_ids=[0])
    return result.results[0]["y"].T.reshape(BATCH, 1)
```
